# Optimizing a Trainium2 kernel written in Bass

```python
import numpy as np
import jax
import jax.numpy as jnp

def _softmax(x, axis=-1):
    return jax.nn.softmax(x, axis=axis)

def _gelu(x):
    return jax.nn.gelu(x, approximate=True)

def _silu(x):
    return jax.nn.silu(x)

def _sigmoid(x):
    return jax.nn.sigmoid(x)

def _layernorm(x, axis=-1, eps=1e-05):
    m = jnp.mean(x, axis=axis, keepdims=True)
    v = jnp.var(x, axis=axis, keepdims=True)
    return (x - m) / jnp.sqrt(v + eps)

def _scatter_add(tgt, idx, src, axis=0):
    return tgt.at[idx].add(src)

def _segment_sum(src, seg, n):
    return jax.ops.segment_sum(src, seg, n)
kernel_name = 'mk_gnn_preln_d1_gnn_r8_0468a0'

def setup_inputs(seed: int=0):
    np.random.seed(seed)
    _w = jnp.asarray

    def _rec_inputs():
        import jax
        import jax.numpy as jnp
        _gk = jax.random.key(seed)
        x = -0.0003713 + 1 * jax.random.normal(jax.random.fold_in(_gk, 1), (12500, 128), jnp.float32)
        _s = jax.random.randint(jax.random.fold_in(_gk, 2), (100000,), 0, 12500, jnp.int32)
        _d = jax.random.randint(jax.random.fold_in(_gk, 3), (100000,), 0, 12500, jnp.int32)
        _loop = jnp.arange(12500, dtype=jnp.int32)
        src = jnp.concatenate([_s, _d, _loop])
        dst = jnp.concatenate([_d, _s, _loop])
        _o = jnp.argsort(dst, stable=True)
        src = src[_o]
        dst = dst[_o]
        return (x, src, dst)
    x, src, dst = _rec_inputs()

    def _L0_gnn_setup():
        import jax, jax.numpy as jnp
        import numpy as np
        N = 12500
        E = 75000
        D_IN = 128
        D = 128
        L = 3

        def gru_cell(m, h, w_ih, w_hh, b_ih, b_hh):
            gi = m @ w_ih.T + b_ih
            gh = h @ w_hh.T + b_hh
            ir, iz, inn = jnp.split(gi, 3, axis=-1)
            hr, hz, hn = jnp.split(gh, 3, axis=-1)
            r = jax.nn.sigmoid(ir + hr)
            z = jax.nn.sigmoid(iz + hz)
            n = jnp.tanh(inn + r * hn)
            return (1.0 - z) * n + z * h
        key = jax.random.key(seed)
        ks = jax.random.split(key, 10)
        s = 1.0 / np.sqrt(D)
        x = jax.random.normal(ks[0], (N, D_IN), dtype=jnp.float32)
        edge_index = jax.random.randint(ks[1], (2, E), 0, N, dtype=jnp.int64)
        lin_w = jax.random.normal(ks[2], (D, D_IN), dtype=jnp.float32) * (1.0 / np.sqrt(D_IN))
        lin_b = jnp.zeros((D,), dtype=jnp.float32)
        weight = jax.random.normal(ks[3], (L, D, D), dtype=jnp.float32) * s
        w_ih = jax.random.normal(ks[4], (3 * D, D), dtype=jnp.float32) * s
        w_hh = jax.random.normal(ks[5], (3 * D, D), dtype=jnp.float32) * s
        b_ih = jnp.zeros((3 * D,), dtype=jnp.float32)
        b_hh = jnp.zeros((3 * D,), dtype=jnp.float32)
        return {'x': x, 'lin_w': lin_w, 'lin_b': lin_b, 'weight': weight, 'w_ih': w_ih, 'w_hh': w_hh, 'b_ih': b_ih, 'b_hh': b_hh, 'edge_index': edge_index}
    _L0_gnn_all = _L0_gnn_setup()
    _L0_gnn_in = {k: v for k, v in _L0_gnn_all.items() if k in ('lin_w', 'lin_b', 'weight', 'w_ih', 'w_hh', 'b_ih', 'b_hh')}
    del _L0_gnn_all
    return {'x': x, 'src': src, 'dst': dst, 'L0_gnn_lin_w': _L0_gnn_in['lin_w'], 'L0_gnn_lin_b': _L0_gnn_in['lin_b'], 'L0_gnn_weight': _L0_gnn_in['weight'], 'L0_gnn_w_ih': _L0_gnn_in['w_ih'], 'L0_gnn_w_hh': _L0_gnn_in['w_hh'], 'L0_gnn_b_ih': _L0_gnn_in['b_ih'], 'L0_gnn_b_hh': _L0_gnn_in['b_hh']}

def reference(x, src, dst, L0_gnn_lin_w, L0_gnn_lin_b, L0_gnn_weight, L0_gnn_w_ih, L0_gnn_w_hh, L0_gnn_b_ih, L0_gnn_b_hh):
    import jax
    import jax.numpy as jnp

    def _L0_gnn_ref(x, lin_w, lin_b, weight, w_ih, w_hh, b_ih, b_hh, edge_index):
        import jax, jax.numpy as jnp
        import numpy as np
        N = 12500
        E = 75000
        D_IN = 128
        D = 128
        L = 3

        def gru_cell(m, h, w_ih, w_hh, b_ih, b_hh):
            gi = m @ w_ih.T + b_ih
            gh = h @ w_hh.T + b_hh
            ir, iz, inn = jnp.split(gi, 3, axis=-1)
            hr, hz, hn = jnp.split(gh, 3, axis=-1)
            r = jax.nn.sigmoid(ir + hr)
            z = jax.nn.sigmoid(iz + hz)
            n = jnp.tanh(inn + r * hn)
            return (1.0 - z) * n + z * h
        h = x @ lin_w.T + lin_b
        src, dst = (edge_index[0], edge_index[1])
        n_nodes = h.shape[0]
        for i in range(weight.shape[0]):
            m = h @ weight[i]
            agg = jax.ops.segment_sum(m[src], dst, num_segments=n_nodes)
            h = gru_cell(agg, h, w_ih, w_hh, b_ih, b_hh)
        return h
    edge_index = jnp.stack([src, dst])
    h = jnp.maximum(_layernorm(x, axis=-1), 0.0)
    x = x + _L0_gnn_ref(h, L0_gnn_lin_w, L0_gnn_lin_b, L0_gnn_weight, L0_gnn_w_ih, L0_gnn_w_hh, L0_gnn_b_ih, L0_gnn_b_hh, edge_index)
    return x

_drawn_inputs = setup_inputs


def setup_inputs(seed=0):
    import zlib

    import numpy as np

    out = dict(_drawn_inputs(seed))
    spreads = {'L0_gnn_lin_b': (0.0, 0.1), 'L0_gnn_b_ih': (0.0, 0.1), 'L0_gnn_b_hh': (0.0, 0.1)}
    factors = {}
    for name, (base, spread) in spreads.items():
        noise = np.random.default_rng([zlib.crc32(name.encode()), seed]).standard_normal(out[name].shape)
        drawn = base * np.exp(spread * noise) if base else spread * noise
        out[name] = jnp.asarray(drawn.astype(out[name].dtype))
    for name, factor in factors.items():
        out[name] = (out[name] * factor).astype(out[name].dtype)
    return out
```

```python
from contextlib import ExitStack

import concourse.bass as bass
from concourse import mybir

P = 128
LAYERS = 3
EPS = 1e-5
TN = 512
TB = TN // P
GC = 8
GE = GC * P
W = 128
RING = 4
IDX_HALVES = 2
PRO = 5

ALU = mybir.AluOpType
ACT = mybir.ActivationFunctionType
AX_X = mybir.AxisListType.X
F32 = mybir.dt.float32
I32 = mybir.dt.int32
RMAX = bass.bass_isa.ReduceOp.max
FAR = 1 << 20
PLAN_STEPS = 6
PLAN_STEPS = 6


def gated_graph_layers(nc, x, src, dst, lin_wT, lin_b, weight, w_ihT, w_hhT, b_ih, b_hh, out, messages):
    NPAD = x.shape[0]
    NT = NPAD // TN
    NG = src.shape[1] // GC
    STEPS = NG // (RING * IDX_HALVES)
    assert NPAD % (TN * PRO) == 0 and NG % (RING * IDX_HALVES) == 0

    with ExitStack() as ctx:
        def sb(name, shape, dt=F32, scope=ctx):
            return scope.enter_context(nc.sbuf_tensor(name, shape, dt))

        def sem(name):
            return ctx.enter_context(nc.semaphore(name))

        hT = sb("hT", [P, NPAD])
        aggT = sb("aggT", [P, NPAD + W])
        edge_src = sb("edge_src", [P, NG * GC], I32)
        edge_rel = sb("edge_rel", [P, NG * GC])
        lowest = sb("lowest", [P, NG])
        plan = sb("plan", [1, 2, NG], I32)
        tile_ready = sb("tile_ready", [1, NT + 1], I32)
        node_iota = sb("node_iota", [P, W])
        ident = sb("ident", [P, P])
        wih = sb("wih", [P, 3 * P])
        whh = sb("whh", [P, 3 * P])
        lin = sb("lin", [P, P])
        wmsg = sb("wmsg", [P, LAYERS * P])
        bias = sb("bias", [P, 3 + 3 + 1])
        bias_rz = sb("bias_rz", [P, 2])
        eps = sb("eps", [P, 1])
        zeros = sb("zeros", [P, TN])
        psum = ctx.enter_context(nc.psum_tensor("psum", [P, 8, TN], F32))

        SUM_CREDIT = IDX_HALVES * RING
        s_edges = sem("edges_loaded")
        s_w = sem("weights_loaded")
        s_const = sem("constants_made")
        s_dst = sem("destination_steps")
        s_ext = sem("group_extremes_on_each_partition")
        s_allext = sem("group_extremes_over_all")
        s_plan = sem("plan_steps")
        s_ready = sem("tile_ready_column")
        s_readyrow = sem("tile_ready_row")
        s_agg0 = sem("aggT_zero")
        s_x = [sem(f"x_loaded_{s}") for s in range(PRO)]
        s_started = sem("groups_started")
        s_seen = sem("statistics_seen")
        s_bn = sem("statistics_ready")
        s_var = sem("variance_ready")
        s_std = sem("std_ready")
        s_rstd = sem("rstd_ready")
        s_xn = sem("x_normed")
        s_xT = sem("x_transposed")
        s_u = sem("relu_ready")
        s_lin = sem("linear_ready")
        s_h0 = sem("h0_ready")
        s_h0T = sem("h0_in_hT")
        s_m0 = sem("first_messages_ready")
        s_m0c = sem("first_messages_copied")
        s_m0free = sem("first_messages_free")
        s_m0st = [sem(f"first_messages_stored_{s}") for s in range(PRO)]
        s_idx = [sem(f"indices_loaded_{h}") for h in range(IDX_HALVES)]
        s_rows = [sem(f"rows_gathered_{r}") for r in range(RING)]
        s_oh = sem("onehot_ready")
        s_sum = sem("group_summed")
        s_add = sem("group_added")
        s_xrel = sem("extra_destinations_shifted")
        s_xoh = sem("extra_onehot_ready")
        s_xsum = sem("extra_window_summed")
        s_xadd = sem("extra_window_added")
        s_gate = sem("gate_products")
        s_r = sem("r_ready")
        s_z = sem("z_ready")
        s_rh = sem("r_times_hn")
        s_npre = sem("n_preactivation")
        s_n = sem("n_ready")
        s_zero = sem("sums_cleared")
        s_blend = sem("blend_steps")
        s_h = sem("h_new_ready")
        s_m = sem("messages_ready")
        s_mc = sem("tile_left_psum")
        s_mst = sem("messages_stored")
        s_xres = sem("residual_loaded")
        s_outst = sem("out_stored")

        pro = ctx.enter_context(ExitStack())
        xin = sb("xin", [P, PRO, TB, P], F32, pro)
        stats = sb("stats", [P, PRO, TB, 6], F32, pro)
        meanvar = sb("meanvar", [P, PRO, TB, 2], F32, pro)
        std = sb("std", [P, PRO, TB], F32, pro)
        rstd = sb("rstd", [P, PRO, TB], F32, pro)
        u = sb("u", [P, PRO, TN], F32, pro)
        h0 = sb("h0", [P, PRO, TN], F32, pro)
        m0 = sb("m0", [P, PRO, TN], F32, pro)
        allext = sb("allext", [P, 2, NG], F32, pro)
        span = sb("span", [1, NG], F32, pro)
        span_i = sb("span_i", [1, NG], I32, pro)
        windows_i = sb("windows_i", [1, NG], I32, pro)
        group_i = sb("group_i", [P, NG], I32, pro)
        group_f = sb("group_f", [P, NG], F32, pro)
        tile_end_i = sb("tile_end_i", [P, 1], I32, pro)
        tile_end = sb("tile_end", [P, 1], F32, pro)
        needs = sb("needs", [NT, NG], F32, pro)
        needed = sb("needed", [NT, 1], F32, pro)
        needed_i = sb("needed_i", [NT, 1], I32, pro)
        iota_i = sb("iota_i", [P, W], I32, pro)
        pro.close()
        assert 2 * NG * GC + 2 * NG <= NPAD
        dst_i = aggT[:, 0:NG * GC].bitcast(I32)
        negdst = aggT[:, NG * GC:2 * NG * GC]
        extremes = aggT[:, 2 * NG * GC:2 * NG * GC + 2 * NG].rearrange("p (k g) -> p k g", k=2)

        idx = sb("idx", [P, IDX_HALVES, RING * GC], I32)
        rows = sb("rows", [P, RING, GC, P])
        onehot = sb("onehot", [P, 2, GC, W])
        xrel = sb("xrel", [P, GC])
        xonehot = sb("xonehot", [P, GC, W])
        gr = sb("gr", [P, TN])
        gz = sb("gz", [P, TN])
        gn = sb("gn", [P, TN])
        npre = sb("npre", [P, TN])
        blend = sb("blend", [P, TN])
        hnew = sb("hnew", [P, TN])
        mst = sb("mst", [P, TN])
        xres = sb("xres", [P, TN])

        GATE_R, GATE_HN, GATE_IN, GATE_Z = (psum[:, b, :] for b in range(4))
        WINDOW = [psum[:, 4 + b, 0:W] for b in range(2)]
        XWINDOW = psum[:, 6, 0:W]
        MSG = psum[:, 7, :]

        def tile_rows(dram, row0):
            return dram[bass.ds(row0, TN), :].rearrange("(b p) d -> p b d", p=P)

        def blocks(ap):
            return ap.rearrange("p (b d) -> p b d", b=TB)

        def staggered(*stages):
            for step in range(PRO + len(stages) - 1):
                for k, stage in enumerate(stages):
                    if 0 <= step - k < PRO:
                        stage(step - k)

        def over_layers(engine, layer_program):
            with engine.Fori(0, LAYERS - 1) as layer:
                layer_program(layer, False)
            layer_program(LAYERS - 1, True)

        block = ctx.enter_context(nc.Block())

        @block.sync
        def _(sp):
            sp.dma_start(edge_src[:], src).then_inc(s_edges, 16)
            sp.dma_start(dst_i, dst).then_inc(s_edges, 16)
            sp.dma_start(lin[:], lin_wT).then_inc(s_w, 16)
            for i in range(LAYERS):
                sp.dma_start(wmsg[:, i * P:(i + 1) * P], weight[i]).then_inc(s_w, 16)
            sp.dma_start(wih[:], w_ihT).then_inc(s_w, 16)
            sp.dma_start(whh[:], w_hhT).then_inc(s_w, 16)
            sp.dma_start(bias[:, 0:3], b_ih).then_inc(s_w, 16)
            sp.dma_start(bias[:, 3:6], b_hh).then_inc(s_w, 16)
            sp.dma_start(bias[:, 6:7], lin_b).then_inc(s_w, 16)
            with sp.Fori(0, NT // PRO) as i:
                for s in range(PRO):
                    sp.wait_ge(s_xT, i * PRO + s + 1)
                    sp.dma_start(xin[:, s], tile_rows(x, (i * PRO + s) * TN)).then_inc(s_x[s], 16)
            sp.wait_ge(s_ready, 1)
            sp.dma_start(tile_ready[0:1, 0:NT], needed_i[:, :]).then_inc(s_readyrow, 16)
            sp.wait_ge(s_readyrow, 16)
            sp.wait_ge(s_h0T, NT + PRO)
            for s in range(PRO):
                sp.wait_ge(s_m0st[s], 16 * (NT // PRO))
            with sp.Fori(0, LAYERS) as layer:
                with sp.Fori(0, STEPS) as i:
                    for h in range(IDX_HALVES):
                        turn = i * IDX_HALVES + h
                        sp.wait_ge(s_sum, layer * NG + (turn + 1 - IDX_HALVES) * RING + SUM_CREDIT)
                        sp.dma_start(idx[:, h, :], edge_src[:, bass.ds(turn * RING * GC, RING * GC)]
                                     ).then_inc(s_idx[h], 16)

        @block.gpsimd
        def _(pool):
            pool.sem_inc(s_h0T, PRO)
            pool.sem_inc(s_m0free, 1)
            nc.gpsimd.memset(ident[:], 0.0).then_inc(s_const, 1)
            pool.wait_ge(s_const, 1)
            nc.gpsimd.affine_select(out=ident[:], in_=ident[:], compare_op=ALU.not_equal, fill=1.0, base=0,
                                    pattern=[[-1, P]], channel_multiplier=1).then_inc(s_const, 1)
            nc.gpsimd.iota(iota_i[:], [[1, W]], base=0, channel_multiplier=0).then_inc(s_const, 1)
            nc.gpsimd.iota(group_i[:], [[1, NG]], base=1, channel_multiplier=0).then_inc(s_const, 1)
            nc.gpsimd.iota(tile_end_i[:], [[0, 1]], base=TN, channel_multiplier=TN).then_inc(s_const, 1)
            nc.gpsimd.memset(eps[:], EPS)
            nc.gpsimd.memset(zeros[:], 0.0).then_inc(s_const, 1)
            nc.gpsimd.memset(tile_ready[:], FAR).then_inc(s_const, 1)
            pool.wait_ge(s_ext, 2)
            nc.gpsimd.partition_all_reduce(allext[:].rearrange("p k g -> p (k g)"),
                                           extremes.rearrange("p k g -> p (k g)"), P, RMAX).then_inc(s_allext, 1)
            pool.wait_ge(s_allext, 1)
            nc.gpsimd.memset(aggT[:], 0.0).then_inc(s_agg0, 1)
            with pool.Fori(0, NT // PRO) as i:
                for s in range(PRO):
                    t = i * PRO + s
                    pool.wait_ge(s_h0, t + 1 + 1)
                    nc.gpsimd.tensor_copy(hT[:, bass.ds(t * TN, TN)], h0[:, s, :]).then_inc(s_h0T, 1)
                    pool.wait_ge(s_m0c, t + 1 + 1)
                    pool.dma_start(tile_rows(messages[0], t * TN), blocks(m0[:, s, :])).then_inc(s_m0st[s], 16)
                for s in range(PRO):
                    pool.wait_ge(s_m0st[s], 16 * (i + 1))
                pool.sem_inc(s_m0free, 1)

            for layer in range(LAYERS):
                if layer:
                    pool.wait_ge(s_mst, 16 * NT * layer)
                with pool.Fori(0, STEPS) as i:
                    for h in range(IDX_HALVES):
                        pool.wait_ge(s_idx[h], 16 * (layer * STEPS + i + 1))
                        for r in range(RING):
                            g = layer * NG + (i * IDX_HALVES + h) * RING + r
                            pool.wait_ge(s_sum, g + 1 - RING + SUM_CREDIT)
                            pool.sem_inc(s_started, 1)
                            for c in range(GC):
                                k = r * GC + c
                                nc.gpsimd.indirect_dma_start(
                                    out=rows[:, r, c, :], out_offset=None, in_=messages[layer],
                                    in_offset=bass.IndirectOffsetOnAxis(ap=idx[:, h, k:k + 1], axis=0),
                                ).then_inc(s_rows[r], 16)

        @block.scalar
        def _(act):
            act.sem_inc(s_u, 1)
            act.sem_inc(s_h0, 1)
            act.sem_inc(s_mc, 1)
            act.wait_ge(s_const, 7)
            act.wait_ge(s_w, 16 * (6 + LAYERS))
            with act.Fori(0, NT // PRO) as i:
                def std_of(s):
                    t = i * PRO + s
                    act.wait_ge(s_var, t + 1)
                    nc.scalar.activation(std[:, s, :], meanvar[:, s, :, 1], ACT.Sqrt, bias=eps[:, 0:1]
                                         ).then_inc(s_std, 1)

                def relu_of(s):
                    t = i * PRO + s
                    act.wait_ge(s_xT, t + 1 + PRO)
                    nc.scalar.activation(u[:, s, :], psum[:, s % 2, :], ACT.Relu).then_inc(s_u, 1)

                def h0_of(s):
                    t = i * PRO + s
                    act.wait_ge(s_lin, t + 1)
                    act.wait_ge(s_h0T, t + 1)
                    nc.scalar.activation(h0[:, s, :], psum[:, 2 + s % 2, :], ACT.Identity, bias=bias[:, 6:7]
                                         ).then_inc(s_h0, 1)

                staggered(std_of, relu_of, h0_of)

            for layer in range(LAYERS):
                last = layer == LAYERS - 1
                with act.Fori(0, NT) as tile:
                    t = layer * NT + tile
                    if last:
                        act.dma_start(blocks(xres[:]), tile_rows(x, tile * TN)).then_inc(s_xres, 16)
                    act.wait_ge(s_gate, 4 * t + 1)
                    nc.scalar.activation(gr[:], GATE_R, ACT.Sigmoid, bias=bias_rz[:, 0:1]).then_inc(s_r, 1)
                    act.wait_ge(s_npre, t + 1)
                    nc.scalar.activation(gn[:], npre[:], ACT.Tanh, bias=bias[:, 2:3]).then_inc(s_n, 1)
                    act.wait_ge(s_gate, 4 * t + 4)
                    nc.scalar.activation(gz[:], GATE_Z, ACT.Sigmoid, bias=bias_rz[:, 1:2]).then_inc(s_z, 1)
                    nc.scalar.copy(aggT[:, bass.ds(tile * TN, TN)], zeros[:]).then_inc(s_zero, 1)
                    if last:
                        act.wait_ge(s_mc, t + 1 + 1)
                        act.dma_start(tile_rows(out, tile * TN), blocks(mst[:])).then_inc(s_outst, 16)
                        act.wait_ge(s_outst, 16 * (tile + 1))
                    else:
                        act.wait_ge(s_h, t + 1)
                        nc.scalar.copy(hT[:, bass.ds(tile * TN, TN)], hnew[:])
                        act.wait_ge(s_m, t + 1)
                        nc.scalar.copy(mst[:], MSG).then_inc(s_mc, 1)
                        act.wait_ge(s_mc, t + 1 + 1)
                        act.dma_start(tile_rows(messages[layer + 1], tile * TN), blocks(mst[:])
                                      ).then_inc(s_mst, 16)
                        act.wait_ge(s_mst, 16 * (t + 1))

        @block.tensor
        def _(pe):
            pe.sem_inc(s_xT, PRO)
            pe.sem_inc(s_sum, SUM_CREDIT)
            pe.wait_ge(s_w, 16 * (6 + LAYERS))
            pe.wait_ge(s_const, 2)
            with pe.Fori(0, NT // PRO) as i:
                def transposes(s):
                    t = i * PRO + s
                    pe.wait_ge(s_xn, t + 1)
                    pe.wait_ge(s_u, t + (s == 0))
                    for b in range(TB):
                        mm = nc.tensor.transpose(psum[:, s % 2, b * P:(b + 1) * P], xin[:, s, b, :], ident[:])
                    mm.then_inc(s_xT, 1)

                def linear(s):
                    t = i * PRO + s
                    pe.wait_ge(s_u, t + 1 + 1)
                    pe.wait_ge(s_h0, t + (s == 0))
                    nc.tensor.matmul(psum[:, 2 + s % 2, :], lin[:], u[:, s, :], start=True, stop=True
                                     ).then_inc(s_lin, 1)

                def messages(s):
                    t = i * PRO + s
                    pe.wait_ge(s_h0, t + 1 + 1)
                    pe.wait_ge(s_m0c, t + (s == 0))
                    for b in range(TB):
                        mm = nc.tensor.matmul(psum[:, 4 + s % 2, b * P:(b + 1) * P], h0[:, s, b * P:(b + 1) * P],
                                              wmsg[:, 0:P], start=True, stop=True)
                    mm.then_inc(s_m0, 1)

                staggered(transposes, linear, messages)

            def update_tile(layer, last, tile, groups_done):
                t = layer * NT + tile
                nodes = bass.ds(tile * TN, TN)
                pe.wait_ge(s_add, groups_done + 1)
                for gate, bank, parts in ((0, GATE_R, "ih"), (2, GATE_HN, "h"), (2, GATE_IN, "i"), (1, GATE_Z, "ih")):
                    cols = slice(gate * P, (gate + 1) * P)
                    if "i" in parts:
                        mm = nc.tensor.matmul(bank, wih[:, cols], aggT[:, nodes], start=True, stop="h" not in parts)
                    if "h" in parts:
                        mm = nc.tensor.matmul(bank, whh[:, cols], hT[:, nodes], start="i" not in parts, stop=True)
                    mm.then_inc(s_gate, 1)
                pe.wait_ge(s_h, t + 1)
                pe.wait_ge(s_mc, t + 1)
                for b in range(TB):
                    cols = slice(b * P, (b + 1) * P)
                    if last:
                        mm = nc.tensor.transpose(MSG[:, cols], hnew[:, cols], ident[:])
                    else:
                        mm = nc.tensor.matmul(MSG[:, cols], hnew[:, cols], wmsg[:, bass.ds((layer + 1) * P, P)],
                                              start=True, stop=True)
                mm.then_inc(s_m, 1)

            extra = pe.alloc_register("extra_windows")
            pe.reg_mov(extra, 0)
            next_tile = pe.alloc_register("next_tile")

            def sum_group(layer, j, r):
                g = j * RING + r
                turn = layer * (NG // RING) + j
                pe.wait_ge(s_rows[r], 16 * GC * (turn + 1))
                windows = pe.value_load(plan[0:1, 1, bass.ds(g, 1)], min_val=1, max_val=NPAD // W)
                with pe.If(windows > 1):
                    with pe.Fori(1, windows):
                        pe.reg_add(extra, extra, 1)
                        pe.wait_ge(s_xoh, pe.snap(extra))
                        for c in range(GC):
                            mm = nc.tensor.matmul(XWINDOW, rows[:, r, c, :], xonehot[:, c, :],
                                                  start=(c == 0), stop=(c == GC - 1))
                        mm.then_inc(s_xsum, 1)
                pe.end_ifs()
                pe.wait_ge(s_oh, layer * NG + g + 1)
                for c in range(GC):
                    mm = nc.tensor.matmul(WINDOW[r % 2], rows[:, r, c, :], onehot[:, r % 2, c, :],
                                          start=(c == 0), stop=(c == GC - 1))
                mm.then_inc(s_sum, 1)

            pe.wait_ge(s_plan, PLAN_STEPS)
            pe.wait_ge(s_readyrow, 16)

            def layer_groups(layer, last):
                pe.reg_mov(next_tile, 0)
                with pe.Fori(0, NG // RING) as j:
                    for r in range(0, RING, 2):
                        sum_group(layer, j, r)
                        sum_group(layer, j, r + 1)
                        done = j * RING + r + 2
                        with pe.While(lambda: pe.value_load(
                                tile_ready[0:1, bass.ds(pe.snap(next_tile, min_val=0, max_val=NT), 1)]) <= done):
                            update_tile(layer, last, pe.snap(next_tile, min_val=0, max_val=NT - 1), layer * NG + done)
                            pe.reg_add(next_tile, next_tile, 1)

            over_layers(pe, layer_groups)

        @block.vector
        def _(dve):
            dve.sem_inc(s_m0c, 1)
            dve.sem_inc(s_add, 1)
            dve.wait_ge(s_edges, 32)
            nc.vector.tensor_copy(edge_rel[:], dst_i).then_inc(s_dst, 1)
            dve.wait_ge(s_dst, 1)
            nc.vector.tensor_scalar(negdst, edge_rel[:], 0.0, -float(FAR), ALU.is_lt, ALU.mult).then_inc(s_dst, 1)
            nc.vector.tensor_reduce(extremes[:, 0, :], edge_rel[:].rearrange("p (g c) -> p g c", c=GC), AX_X, ALU.max
                                    ).then_inc(s_ext, 1)
            dve.wait_ge(s_dst, 2)
            nc.vector.tensor_tensor(negdst, negdst, edge_rel[:], ALU.subtract).then_inc(s_dst, 1)
            dve.wait_ge(s_dst, 3)
            nc.vector.tensor_reduce(extremes[:, 1, :], negdst.rearrange("p (g c) -> p g c", c=GC), AX_X, ALU.max
                                    ).then_inc(s_ext, 1)
            dve.wait_ge(s_w, 16 * (6 + LAYERS))
            nc.vector.tensor_tensor(bias_rz[:], bias[:, 0:2], bias[:, 3:5], ALU.add)
            dve.wait_ge(s_const, 7)
            nc.vector.tensor_copy(node_iota[:], iota_i[:])
            nc.vector.tensor_copy(group_f[:], group_i[:])
            nc.vector.tensor_copy(tile_end[:], tile_end_i[:]).then_inc(s_dst, 1)

            with dve.Fori(0, NT // PRO) as i:
                def statistics(s):
                    t = i * PRO + s
                    dve.wait_ge(s_x[s], 16 * (i + 1))
                    for b in range(TB):
                        st = nc.vector.bn_stats(stats[:, s, b, :], xin[:, s, b, :])
                    st.then_inc(s_bn, 1)
                    dve.wait_ge(s_bn, t + 1)
                    dve.sem_inc(s_seen, 1)
                    for b in range(TB):
                        ag = nc.vector.bn_aggr(meanvar[:, s, b, :], stats[:, s, b, :])
                    ag.then_inc(s_var, 1)

                def normed(s):
                    t = i * PRO + s
                    dve.wait_ge(s_std, t + 1)
                    nc.vector.reciprocal(rstd[:, s, :], std[:, s, :]).then_inc(s_rstd, 1)
                    dve.wait_ge(s_rstd, t + 1)
                    for b in range(TB):
                        xn = nc.vector.tensor_scalar(xin[:, s, b, :], xin[:, s, b, :], meanvar[:, s, b, 0:1],
                                                     rstd[:, s, b:b + 1], ALU.subtract, ALU.mult)
                    xn.then_inc(s_xn, 1)

                def messages_out(s):
                    t = i * PRO + s
                    dve.wait_ge(s_m0, t + 1)
                    dve.wait_ge(s_m0free, i + 1)
                    nc.vector.tensor_copy(m0[:, s, :], psum[:, 4 + s % 2, :]).then_inc(s_m0c, 1)

                staggered(statistics, normed, lambda s: None, messages_out)

            dve.wait_ge(s_allext, 1)
            dve.wait_ge(s_dst, 4)
            nc.vector.tensor_scalar(lowest[:], allext[:, 1, :], -1.0, None, ALU.mult).then_inc(s_plan, 1)
            nc.vector.tensor_tensor(span[:], allext[0:1, 0, :], allext[0:1, 1, :], ALU.add).then_inc(s_plan, 1)
            dve.wait_ge(s_plan, 2)
            nc.vector.tensor_copy(plan[:, 0, :], lowest[0:1, :])
            nc.vector.tensor_copy(span_i[:], span[:]).then_inc(s_plan, 1)
            rel = edge_rel[:].rearrange("p (g c) -> p g c", c=GC)
            nc.vector.tensor_tensor(rel, rel, lowest[:].unsqueeze(2).to_broadcast([P, NG, GC]), ALU.subtract)
            nc.vector.scalar_tensor_tensor(needs[:], lowest[0:NT, :], tile_end[0:NT, 0:1], group_f[0:NT, :],
                                           ALU.is_lt, ALU.mult).then_inc(s_plan, 1)
            dve.wait_ge(s_plan, 4)
            nc.vector.tensor_scalar(windows_i[:], span_i[:], W.bit_length() - 1, None, ALU.logical_shift_right)
            nc.vector.tensor_reduce(needed[:], needs[:], AX_X, ALU.max).then_inc(s_plan, 1)
            dve.wait_ge(s_plan, 5)
            nc.vector.tensor_scalar(plan[:, 1, :], windows_i[:], 1, None, ALU.add).then_inc(s_plan, 1)
            nc.vector.tensor_copy(needed_i[:], needed[:]).then_inc(s_ready, 1)
            dve.wait_ge(s_plan, PLAN_STEPS)
            dve.wait_ge(s_readyrow, 16)
            dve.wait_ge(s_agg0, 1)
            dve.wait_ge(s_h0T, NT + PRO)
            for s in range(PRO):
                dve.wait_ge(s_m0st[s], 16 * (NT // PRO))

            extra = dve.alloc_register("extra_windows")
            shifts = dve.alloc_register("extra_shifts")
            dve.reg_mov(extra, 0)
            dve.reg_mov(shifts, 0)
            next_tile = dve.alloc_register("next_tile")
            extra_low = dve.alloc_register("extra_window_low")
            columns = node_iota[:].unsqueeze(1).to_broadcast([P, GC, W])

            def window_onehot(out_, rel_):
                return nc.vector.tensor_tensor(out_, rel_.unsqueeze(2).to_broadcast([P, GC, W]), columns,
                                               ALU.is_equal)

            def make_onehot(layer, j, r):
                g = j * RING + r
                rel_g = edge_rel[:, bass.ds(g * GC, GC)]
                windows = dve.value_load(plan[0:1, 1, bass.ds(g, 1)], min_val=1, max_val=NPAD // W)
                with dve.If(windows > 1):
                    low = dve.value_load(plan[0:1, 0, bass.ds(g, 1)], min_val=0, max_val=NPAD - 1)
                    dve.reg_mov(extra_low, low)
                    dve.wait_ge(s_add, layer * NG + (j * RING + r - r % 2) + 1)
                    dve.reg_add(shifts, shifts, 1)
                    nc.vector.tensor_copy(xrel[:], rel_g).then_inc(s_xrel, 1)
                    with dve.Fori(1, windows):
                        dve.wait_ge(s_xrel, dve.snap(shifts))
                        dve.reg_add(shifts, shifts, 1)
                        nc.vector.tensor_scalar(xrel[:], xrel[:], -float(W), None, ALU.add).then_inc(s_xrel, 1)
                        dve.wait_ge(s_xrel, dve.snap(shifts))
                        window_onehot(xonehot[:], xrel[:]).then_inc(s_xoh, 1)
                        dve.reg_add(extra, extra, 1)
                        dve.wait_ge(s_xsum, dve.snap(extra))
                        dve.reg_add(extra_low, extra_low, W)
                        cols = aggT[:, bass.ds(dve.snap(extra_low, min_val=W, max_val=NPAD), W)]
                        nc.vector.tensor_tensor(cols, cols, XWINDOW, ALU.add).then_inc(s_xadd, 1)
                        dve.wait_ge(s_xadd, dve.snap(extra))
                dve.end_ifs()
                window_onehot(onehot[:, r % 2], rel_g).then_inc(s_oh, 1)

            def add_group(layer, j, r):
                g = j * RING + r
                low = dve.value_load(plan[0:1, 0, bass.ds(g, 1)], min_val=0, max_val=NPAD - 1)
                cols = aggT[:, bass.ds(low, W)]
                dve.wait_ge(s_sum, layer * NG + g + 1 + SUM_CREDIT)
                dve.wait_ge(s_add, layer * NG + g + 1)
                nc.vector.tensor_tensor(cols, cols, WINDOW[r % 2], ALU.add).then_inc(s_add, 1)

            def update_tile(layer, last, tile):
                t = layer * NT + tile
                nodes = bass.ds(tile * TN, TN)
                dve.wait_ge(s_gate, 4 * t + 2)
                dve.wait_ge(s_r, t + 1)
                nc.vector.scalar_tensor_tensor(blend[:], GATE_HN, bias[:, 5:6], gr[:], ALU.add, ALU.mult
                                               ).then_inc(s_rh, 1)
                dve.wait_ge(s_rh, t + 1)
                dve.wait_ge(s_gate, 4 * t + 3)
                nc.vector.tensor_tensor(npre[:], blend[:], GATE_IN, ALU.add).then_inc(s_npre, 1)
                dve.wait_ge(s_n, t + 1)
                nc.vector.tensor_tensor(blend[:], hT[:, nodes], gn[:], ALU.subtract).then_inc(s_blend, 1)
                dve.wait_ge(s_blend, 2 * t + 1)
                dve.wait_ge(s_z, t + 1)
                nc.vector.tensor_tensor(blend[:], blend[:], gz[:], ALU.mult).then_inc(s_blend, 1)
                dve.wait_ge(s_blend, 2 * t + 2)
                dve.wait_ge(s_mc, t + 1)
                nc.vector.tensor_tensor(hnew[:], blend[:], gn[:], ALU.add).then_inc(s_h, 1)
                dve.wait_ge(s_zero, t + 1)
                if last:
                    dve.wait_ge(s_m, t + 1)
                    dve.wait_ge(s_xres, 16 * (tile + 1))
                    nc.vector.tensor_tensor(mst[:], MSG, xres[:], ALU.add).then_inc(s_mc, 1)

            def layer_groups(layer, last):
                dve.reg_mov(next_tile, 0)
                with dve.Fori(0, NG // RING) as j:
                    for r in range(0, RING, 2):
                        make_onehot(layer, j, r)
                        make_onehot(layer, j, r + 1)
                        add_group(layer, j, r)
                        add_group(layer, j, r + 1)
                        done = j * RING + r + 2
                        with dve.While(lambda: dve.value_load(
                                tile_ready[0:1, bass.ds(dve.snap(next_tile, min_val=0, max_val=NT), 1)]) <= done):
                            update_tile(layer, last, dve.snap(next_tile, min_val=0, max_val=NT - 1))
                            dve.reg_add(next_tile, next_tile, 1)

            over_layers(dve, layer_groups)


def kernel(x, src, dst, L0_gnn_lin_w, L0_gnn_lin_b, L0_gnn_weight, L0_gnn_w_ih, L0_gnn_w_hh, L0_gnn_b_ih,
           L0_gnn_b_hh):
    import numpy as np
    import concourse.bacc as bacc
    from concourse.bass_utils import run_bass_kernel_spmd

    x = np.asarray(x)
    N, D = x.shape
    E = src.shape[0]
    whole = -(-N // (TN * PRO)) * TN * PRO
    x_rows = np.zeros((whole, D), x.dtype)
    x_rows[:N] = x
    unit = GE * RING * IDX_HALVES
    edges = -(-E // unit) * unit

    def by_group(a, pad):
        whole = np.full(edges, pad, np.int32)
        whole[:E] = np.asarray(a)
        return np.ascontiguousarray(whole.reshape(edges // GE, P, GC).transpose(1, 0, 2).reshape(P, -1))

    def columns(b):
        return np.ascontiguousarray(np.asarray(b).reshape(-1, P).T)

    arrays = {
        "x": x_rows,
        "src": by_group(src, 0),
        "dst": by_group(dst, -1),
        "lin_wT": np.ascontiguousarray(np.asarray(L0_gnn_lin_w).T),
        "lin_b": columns(L0_gnn_lin_b),
        "weight": np.ascontiguousarray(L0_gnn_weight),
        "w_ihT": np.ascontiguousarray(np.asarray(L0_gnn_w_ih).T),
        "w_hhT": np.ascontiguousarray(np.asarray(L0_gnn_w_hh).T),
        "b_ih": columns(L0_gnn_b_ih),
        "b_hh": columns(L0_gnn_b_hh),
    }
    nc = bacc.Bacc("TRN2", target_bir_lowering=False, num_devices=1)
    args = {n: nc.dram_tensor(f"in_{n}", a.shape, mybir.dt.from_np(a.dtype), kind="ExternalInput").ap()
            for n, a in arrays.items()}
    args["messages"] = [nc.dram_tensor(f"messages_{i}", (whole, D), F32, kind="Internal").ap() for i in range(LAYERS)]
    args["out"] = nc.dram_tensor("out_rows", (whole, D), F32, kind="ExternalOutput").ap()
    gated_graph_layers(nc, **args)
    r = run_bass_kernel_spmd(nc, [{f"in_{n}": a for n, a in arrays.items()}], core_ids=[0])
    return r.results[0]["out_rows"][:N]
```

```python
from contextlib import ExitStack

import concourse.bass as bass
from concourse import mybir

P = 128
EPS = 1e-5
TN = 256
TB = TN // P
GC = 8
GE = GC * P
W = 128
RING = 4
PARTS = ((0, 6), (6, 8))
IDX_HALVES = 2
PTN = 512
PTB = PTN // P
PRO = 5

ALU = mybir.AluOpType
ACT = mybir.ActivationFunctionType
AX_X = mybir.AxisListType.X
F32 = mybir.dt.float32
I32 = mybir.dt.int32
RMAX = bass.bass_isa.ReduceOp.max
FAR = 1 << 20
PLAN_STEPS = 6


def gated_graph_layers(nc, x, src, dst, lin_wT, lin_b, weight, w_ihT, w_hhT, b_ih, b_hh, out, messages):
    LAYERS = weight.shape[0]
    NPAD = x.shape[0]
    NT = out.shape[0] // TN
    PASSES = NPAD // (PTN * PRO)
    NG = src.shape[1] // GC
    STEPS = NG // (RING * IDX_HALVES)
    assert PASSES > 2 and NPAD % (PTN * PRO) == 0 and NG % (RING * IDX_HALVES) == 0 and out.shape[0] % TN == 0
    assert (NT + 1) * TN <= NPAD

    with ExitStack() as ctx:
        def sb(name, shape, dt=F32, scope=ctx):
            return scope.enter_context(nc.sbuf_tensor(name, shape, dt))

        def sem(name):
            return ctx.enter_context(nc.semaphore(name))

        hT = sb("hT", [P, NPAD])
        aggT = sb("aggT", [P, NPAD + W])
        edge_src = sb("edge_src", [P, NG * GC], I32)
        edge_rel = sb("edge_rel", [P, NG * GC])
        dst_i = sb("dst_i", [P, NG * GC], I32)
        real_dst = dst_i[:].bitcast(F32)
        lowest = sb("lowest", [P, NG])
        plan = sb("plan", [1, 2, NG], I32)
        tile_ready = sb("tile_ready", [1, NT + 1], I32)
        node_iota = sb("node_iota", [P, W])
        ident = sb("ident", [P, P])
        wih = sb("wih", [P, 3 * P])
        whh = sb("whh", [P, 3 * P])
        lin = sb("lin", [P, P])
        wmsg = sb("wmsg", [P, LAYERS * P])
        bias = sb("bias", [P, 3 + 3 + 1])
        bias_rz = sb("bias_rz", [P, 2])
        eps = sb("eps", [P, 1])
        zeros = sb("zeros", [P, TN])
        idx = sb("idx", [P, IDX_HALVES, RING * GC], I32)
        extremes = sb("extremes", [P, 2, NG])
        allext = sb("allext", [P, 2, NG])
        span = sb("span", [1, NG])
        span_i = sb("span_i", [1, NG], I32)
        windows_i = sb("windows_i", [1, NG], I32)
        group_i = sb("group_i", [P, NG], I32)
        group_f = sb("group_f", [P, NG])
        tile_end_i = sb("tile_end_i", [P, 1], I32)
        tile_end = sb("tile_end", [P, 1])
        needs = sb("needs", [NT, NG])
        needed = sb("needed", [NT, 1])
        needed_i = sb("needed_i", [NT, 1], I32)
        iota_i = sb("iota_i", [P, W], I32)
        psum = ctx.enter_context(nc.psum_tensor("psum", [P, 8, PTN], F32))

        SUM_CREDIT = IDX_HALVES * RING
        s_brz = sem("bias_rz_ready")
        s_src = sem("src_loaded")
        s_dstl = sem("dst_loaded")
        s_w = sem("weights_loaded")
        s_const = sem("constants_made")
        s_dst = sem("destination_steps")
        s_ext = sem("group_extremes_on_each_partition")
        s_allext = sem("group_extremes_over_all")
        s_plan = sem("plan_steps")
        s_ready = sem("tile_ready_column")
        s_readyrow = sem("tile_ready_row")
        s_agg0 = sem("aggT_zero")
        s_xl = [sem(f"x_loaded_{i}") for i in range(PASSES)]
        s_x = sem("x_passes_loaded")
        s_seen = sem("statistics_seen")
        s_started = sem("groups_started")
        s_bn = sem("statistics_ready")
        s_var = sem("variance_ready")
        s_std = sem("std_ready")
        s_rstd = sem("rstd_ready")
        s_xn = sem("x_normed")
        s_xT = sem("x_transposed")
        s_u = sem("relu_ready")
        s_lin = sem("linear_ready")
        s_h0 = sem("h0_ready")
        s_m0 = sem("first_messages_ready")
        s_m0c = sem("first_messages_copied")
        s_h0T = [sem(f"h0_in_hT_{s}") for s in range(PRO)]
        s_m0st = [sem(f"first_messages_stored_{s}") for s in range(PRO)]
        s_idx = [sem(f"indices_loaded_{h}") for h in range(IDX_HALVES)]
        s_rows = [[sem(f"rows_gathered_{r}_{k}") for k in range(len(PARTS))] for r in range(RING)]
        s_oh = sem("onehot_ready")
        s_sum = sem("group_summed")
        s_add = sem("group_added")
        s_xrel = sem("extra_destinations_shifted")
        s_xoh = sem("extra_onehot_ready")
        s_xsum = sem("extra_window_summed")
        s_xadd = sem("extra_window_added")
        s_hn = sem("state_products")
        s_gate = sem("gate_products")
        s_r = sem("r_ready")
        s_z = sem("z_ready")
        s_rh = sem("r_times_hn")
        s_npre = sem("n_preactivation")
        s_n = sem("n_ready")
        s_zero = sem("sums_cleared")
        s_blend = sem("blend_steps")
        s_h = sem("h_new_ready")
        s_m = sem("messages_ready")
        s_mc = sem("tile_left_psum")
        s_mst = sem("messages_stored")
        s_xres = sem("residual_loaded")
        s_outst = sem("out_stored")

        pro = ctx.enter_context(ExitStack())
        stats = sb("stats", [P, PRO, PTB, 6], F32, pro)
        meanvar = sb("meanvar", [P, PRO, PTB, 2], F32, pro)
        std = sb("std", [P, PRO, PTB], F32, pro)
        rstd = sb("rstd", [P, PRO, PTB], F32, pro)
        xn = sb("xn", [P, PRO, PTN], F32, pro)
        u = sb("u", [P, PRO, PTN], F32, pro)
        h0 = sb("h0", [P, PRO, PTN], F32, pro)
        m0 = sb("m0", [P, PRO, PTN], F32, pro)
        pro.close()

        rows = sb("rows", [P, RING, GC, P])
        onehot = sb("onehot", [P, 2, GC, W])
        xrel = sb("xrel", [P, GC])
        xonehot = sb("xonehot", [P, GC, W])
        gr = sb("gr", [P, TN])
        gz = sb("gz", [P, TN])
        gn = sb("gn", [P, TN])
        npre = sb("npre", [P, TN])
        blend = sb("blend", [P, TN])
        hnew = sb("hnew", [P, TN])
        mst = sb("mst", [P, TN])
        xres = sb("xres", [P, TN])

        GATE_R, GATE_HN, GATE_IN, GATE_Z = (psum[:, b, 0:TN] for b in range(4))
        WINDOW = [psum[:, 4 + b, 0:W] for b in range(2)]
        XWINDOW = psum[:, 6, 0:W]
        MSG = psum[:, 7, 0:TN]

        def tile_rows(dram, row0, n=TN):
            return dram[bass.ds(row0, n), :].rearrange("(b p) d -> p b d", p=P)

        def blocks(ap):
            return ap.rearrange("p (b d) -> p b d", d=P)

        def staggered(*stages, between=None):
            for step in range(PRO + len(stages) - 1):
                if step == PRO and between:
                    between()
                for k, stage in enumerate(stages):
                    if 0 <= step - k < PRO:
                        stage(step - k)

        def over_passes(engine, one_pass):
            one_pass(0)
            with engine.Fori(1, PASSES - 1) as i:
                one_pass(i)
            one_pass(PASSES - 1)

        def later(i):
            return not (isinstance(i, int) and i == 0)

        def prologue_scratch_free(engine):
            for s in range(PRO):
                engine.wait_ge(s_h0T[s], 16 * PASSES)
                engine.wait_ge(s_m0st[s], 16 * PASSES)

        def over_layers(engine, layer_program):
            with engine.Fori(0, LAYERS - 1) as layer:
                layer_program(layer, False)
            layer_program(LAYERS - 1, True)

        block = ctx.enter_context(nc.Block())

        @block.sync
        def _(sp):
            for i in range(PASSES):
                sp.dma_start(blocks(hT[:, i * PRO * PTN:(i + 1) * PRO * PTN]), tile_rows(x, i * PRO * PTN, PRO * PTN)
                             ).then_inc(s_xl[i], 16)
                if i == 0:
                    sp.dma_start(lin[:], lin_wT).then_inc(s_w, 16)
                    sp.dma_start(bias[:, 6:7], lin_b).then_inc(s_w, 16)
                    for k in range(LAYERS):
                        sp.dma_start(wmsg[:, k * P:(k + 1) * P], weight[k]).then_inc(s_w, 16)
                    sp.dma_start(wih[:], w_ihT).then_inc(s_w, 16)
                    sp.dma_start(whh[:], w_hhT).then_inc(s_w, 16)
                    sp.dma_start(bias[:, 0:3], b_ih).then_inc(s_w, 16)
                    sp.dma_start(bias[:, 3:6], b_hh).then_inc(s_w, 16)
            sp.dma_start(dst_i[:], dst).then_inc(s_dstl, 16)
            sp.dma_start(edge_src[:], src).then_inc(s_src, 16)
            for i in range(PASSES):
                sp.wait_ge(s_xl[i], 16)
                sp.sem_inc(s_x, 1)

            def results_out(i):
                def h0_out(s):
                    t = i * PRO + s
                    sp.wait_ge(s_h0, t + 1)
                    sp.dma_start(hT[:, bass.ds(t * PTN, PTN)], h0[:, s, :]).then_inc(s_h0T[s], 16)

                def m0_out(s):
                    t = i * PRO + s
                    sp.wait_ge(s_m0c, t + 1)
                    sp.dma_start(tile_rows(messages[0], t * PTN, PTN), blocks(m0[:, s, :])).then_inc(s_m0st[s], 16)

                staggered(h0_out, m0_out)

            over_passes(sp, results_out)

            def tile_ready_row():
                sp.wait_ge(s_ready, 1)
                sp.dma_start(tile_ready[0:1, 0:NT], needed_i[:, :]).then_inc(s_readyrow, 16)

            def indices(layer, i):
                for h in range(IDX_HALVES):
                    turn = i * IDX_HALVES + h
                    sp.wait_ge(s_sum, layer * NG + (turn + 1 - IDX_HALVES) * RING + SUM_CREDIT)
                    sp.dma_start(idx[:, h, :], edge_src[:, bass.ds(turn * RING * GC, RING * GC)]
                                 ).then_inc(s_idx[h], 16)

            sp.wait_ge(s_src, 16)
            indices(0, 0)
            tile_ready_row()
            with sp.Fori(1, STEPS) as i:
                indices(0, i)
            with sp.Fori(1, LAYERS) as layer:
                with sp.Fori(0, STEPS) as i:
                    indices(layer, i)

        @block.gpsimd
        def _(pool):
            nc.gpsimd.memset(ident[:], 0.0).then_inc(s_const, 1)
            pool.wait_ge(s_const, 1)
            nc.gpsimd.affine_select(out=ident[:], in_=ident[:], compare_op=ALU.not_equal, fill=1.0, base=0,
                                    pattern=[[-1, P]], channel_multiplier=1).then_inc(s_const, 1)
            nc.gpsimd.iota(iota_i[:], [[1, W]], base=0, channel_multiplier=0).then_inc(s_const, 1)
            nc.gpsimd.iota(group_i[:], [[1, NG]], base=1, channel_multiplier=0).then_inc(s_const, 1)
            nc.gpsimd.iota(tile_end_i[:], [[0, 1]], base=TN, channel_multiplier=TN).then_inc(s_const, 1)
            nc.gpsimd.memset(eps[:], EPS)
            nc.gpsimd.memset(zeros[:], 0.0).then_inc(s_const, 1)
            nc.gpsimd.memset(tile_ready[:], FAR).then_inc(s_const, 1)
            nc.gpsimd.memset(aggT[:], 0.0).then_inc(s_agg0, 1)
            pool.wait_ge(s_ext, 2)
            nc.gpsimd.partition_all_reduce(allext[:].rearrange("p k g -> p (k g)"),
                                           extremes[:].rearrange("p k g -> p (k g)"), P, RMAX).then_inc(s_allext, 1)
            prologue_scratch_free(pool)

            for layer in range(LAYERS):
                if layer:
                    pool.wait_ge(s_mst, 16 * NT * layer)
                with pool.Fori(0, STEPS) as i:
                    for h in range(IDX_HALVES):
                        pool.wait_ge(s_idx[h], 16 * (layer * STEPS + i + 1))
                        for r in range(RING):
                            g = layer * NG + (i * IDX_HALVES + h) * RING + r
                            pool.wait_ge(s_sum, g + 1 - RING + SUM_CREDIT)
                            pool.sem_inc(s_started, 1)
                            for part, (c0, c1) in enumerate(PARTS):
                                for c in range(c0, c1):
                                    k = r * GC + c
                                    nc.gpsimd.indirect_dma_start(
                                        out=rows[:, r, c, :], out_offset=None, in_=messages[layer],
                                        in_offset=bass.IndirectOffsetOnAxis(ap=idx[:, h, k:k + 1], axis=0),
                                    ).then_inc(s_rows[r][part], 16)

        @block.scalar
        def _(act):
            act.sem_inc(s_mc, 1)
            act.wait_ge(s_const, 7)
            act.wait_ge(s_w, 16 * (6 + LAYERS))

            def std_of(i):
                act.wait_ge(s_var, i + 1)
                nc.scalar.activation(std[:], meanvar[:, :, :, 1], ACT.Sqrt, bias=eps[:, 0:1]).then_inc(s_std, 1)

            def one_pass(i):
                last = isinstance(i, int) and i == PASSES - 1

                def relu_of(s):
                    act.wait_ge(s_xT, i * PRO + s + 1)
                    nc.scalar.activation(u[:, s, :], psum[:, s % 2, :], ACT.Relu).then_inc(s_u, 1)

                def h0_of(s):
                    act.wait_ge(s_lin, i * PRO + s + 1)
                    if later(i):
                        act.wait_ge(s_h0T[s], 16 * i)
                    nc.scalar.activation(h0[:, s, :], psum[:, 2 + s % 2, :], ACT.Identity, bias=bias[:, 6:7]
                                         ).then_inc(s_h0, 1)

                def m0_of(s):
                    act.wait_ge(s_m0, i * PRO + s + 1)
                    if later(i):
                        act.wait_ge(s_m0st[s], 16 * i)
                    nc.scalar.copy(m0[:, s, :], psum[:, 4 + s % 2, :]).then_inc(s_m0c, 1)

                staggered(relu_of, h0_of, m0_of, between=None if last else lambda: std_of(i + 1))

            std_of(0)
            over_passes(act, one_pass)
            act.wait_ge(s_brz, 1)
            act.wait_ge(s_const, 7)
            prologue_scratch_free(act)

            for layer in range(LAYERS):
                last = layer == LAYERS - 1
                with act.Fori(0, NT) as tile:
                    t = layer * NT + tile
                    if last:
                        act.dma_start(blocks(xres[:]), tile_rows(x, tile * TN)).then_inc(s_xres, 16)
                    act.wait_ge(s_gate, 3 * t + 1)
                    nc.scalar.activation(gr[:], GATE_R, ACT.Sigmoid, bias=bias_rz[:, 0:1]).then_inc(s_r, 1)
                    act.wait_ge(s_npre, t + 1)
                    nc.scalar.activation(gn[:], npre[:], ACT.Tanh, bias=bias[:, 2:3]).then_inc(s_n, 1)
                    act.wait_ge(s_gate, 3 * t + 3)
                    nc.scalar.activation(gz[:], GATE_Z, ACT.Sigmoid, bias=bias_rz[:, 1:2]).then_inc(s_z, 1)
                    nc.scalar.copy(aggT[:, bass.ds(tile * TN, TN)], zeros[:]).then_inc(s_zero, 1)
                    if last:
                        act.wait_ge(s_mc, t + 1 + 1)
                        act.dma_start(tile_rows(out, tile * TN), blocks(mst[:])).then_inc(s_outst, 16)
                        act.wait_ge(s_outst, 16 * (tile + 1))
                    else:
                        act.wait_ge(s_h, t + 1)
                        nc.scalar.copy(hT[:, bass.ds(tile * TN, TN)], hnew[:])
                        act.wait_ge(s_m, t + 1)
                        nc.scalar.copy(mst[:], MSG).then_inc(s_mc, 1)
                        act.wait_ge(s_mc, t + 1 + 1)
                        act.dma_start(tile_rows(messages[layer + 1], tile * TN), blocks(mst[:])
                                      ).then_inc(s_mst, 16)
                        act.wait_ge(s_mst, 16 * (t + 1))

        @block.tensor
        def _(pe):
            pe.sem_inc(s_sum, SUM_CREDIT)
            pe.wait_ge(s_w, 16 * (6 + LAYERS))
            pe.wait_ge(s_const, 2)

            def one_pass(i):
                def bank_read(count, s):
                    if s >= 2:
                        pe.wait_ge(count, i * PRO + s - 1)
                    elif later(i):
                        pe.wait_ge(count, i * PRO - (s == 1))

                def transposes(s):
                    pe.wait_ge(s_xn, i * PRO + s + 1)
                    bank_read(s_u, s)
                    for b in range(PTB):
                        mm = nc.tensor.transpose(psum[:, s % 2, b * P:(b + 1) * P], xn[:, s, b * P:(b + 1) * P],
                                                 ident[:])
                    mm.then_inc(s_xT, 1)

                def linear(s):
                    pe.wait_ge(s_u, i * PRO + s + 1)
                    bank_read(s_h0, s)
                    nc.tensor.matmul(psum[:, 2 + s % 2, :], lin[:], u[:, s, :], start=True, stop=True
                                     ).then_inc(s_lin, 1)

                def messages_of(s):
                    pe.wait_ge(s_h0, i * PRO + s + 1)
                    bank_read(s_m0c, s)
                    for b in range(PTB):
                        mm = nc.tensor.matmul(psum[:, 4 + s % 2, b * P:(b + 1) * P], h0[:, s, b * P:(b + 1) * P],
                                              wmsg[:, 0:P], start=True, stop=True)
                    mm.then_inc(s_m0, 1)

                staggered(transposes, linear, messages_of)

            over_passes(pe, one_pass)

            def state_products(tile):
                nodes = bass.ds(tile * TN, TN)
                nc.tensor.matmul(GATE_R, whh[:, 0:P], hT[:, nodes], start=True, stop=True)
                nc.tensor.matmul(GATE_Z, whh[:, P:2 * P], hT[:, nodes], start=True, stop=True)
                nc.tensor.matmul(GATE_HN, whh[:, 2 * P:3 * P], hT[:, nodes], start=True, stop=True
                                 ).then_inc(s_hn, 1)

            def update_tile(layer, last, tile, groups_done):
                t = layer * NT + tile
                nodes = bass.ds(tile * TN, TN)
                pe.wait_ge(s_add, groups_done + 1)
                for gate, bank, alone in ((0, GATE_R, False), (2, GATE_IN, True), (1, GATE_Z, False)):
                    nc.tensor.matmul(bank, wih[:, gate * P:(gate + 1) * P], aggT[:, nodes], start=alone, stop=True,
                                     skip_group_check=not alone).then_inc(s_gate, 1)
                pe.wait_ge(s_h, t + 1)
                pe.wait_ge(s_mc, t + 1)
                for b in range(TB):
                    cols = slice(b * P, (b + 1) * P)
                    if last:
                        mm = nc.tensor.transpose(MSG[:, cols], hnew[:, cols], ident[:])
                    else:
                        mm = nc.tensor.matmul(MSG[:, cols], hnew[:, cols], wmsg[:, bass.ds((layer + 1) * P, P)],
                                              start=True, stop=True)
                mm.then_inc(s_m, 1)
                state_products(tile + 1)

            extra = pe.alloc_register("extra_windows")
            pe.reg_mov(extra, 0)
            next_tile = pe.alloc_register("next_tile")

            def sum_group(layer, j, r):
                g = j * RING + r
                turn = layer * (NG // RING) + j
                windows = pe.value_load(plan[0:1, 1, bass.ds(g, 1)], min_val=1, max_val=NPAD // W)
                with pe.If(windows > 1):
                    with pe.Fori(1, windows):
                        pe.reg_add(extra, extra, 1)
                        pe.wait_ge(s_xoh, pe.snap(extra))
                        for part, (c0, c1) in enumerate(PARTS):
                            pe.wait_ge(s_rows[r][part], 16 * (c1 - c0) * (turn + 1))
                        for c in range(GC):
                            mm = nc.tensor.matmul(XWINDOW, rows[:, r, c, :], xonehot[:, c, :],
                                                  start=(c == 0), stop=(c == GC - 1))
                        mm.then_inc(s_xsum, 1)
                pe.end_ifs()
                pe.wait_ge(s_oh, layer * NG + g + 1)
                for part, (c0, c1) in enumerate(PARTS):
                    pe.wait_ge(s_rows[r][part], 16 * (c1 - c0) * (turn + 1))
                    for c in range(c0, c1):
                        mm = nc.tensor.matmul(WINDOW[r % 2], rows[:, r, c, :], onehot[:, r % 2, c, :],
                                              start=(c == 0), stop=(c == GC - 1))
                mm.then_inc(s_sum, 1)

            pe.wait_ge(s_m0c, PRO * PASSES)
            prologue_scratch_free(pe)
            pe.wait_ge(s_plan, PLAN_STEPS)
            pe.wait_ge(s_readyrow, 16)

            def layer_groups(layer, last):
                pe.reg_mov(next_tile, 0)
                state_products(0)
                with pe.Fori(0, NG // RING) as j:
                    for r in range(0, RING, 2):
                        sum_group(layer, j, r)
                        sum_group(layer, j, r + 1)
                        done = j * RING + r + 2
                        with pe.While(lambda: pe.value_load(
                                tile_ready[0:1, bass.ds(pe.snap(next_tile, min_val=0, max_val=NT), 1)]) <= done):
                            update_tile(layer, last, pe.snap(next_tile, min_val=0, max_val=NT - 1), layer * NG + done)
                            pe.reg_add(next_tile, next_tile, 1)

            over_layers(pe, layer_groups)

        @block.vector
        def _(dve):
            dve.sem_inc(s_add, 1)

            def one_pass(i):
                dve.wait_ge(s_x, i + 1)
                x_pass = [hT[:, bass.ds((i * PRO + s) * PTN + b * P, P)] for s in range(PRO) for b in range(PTB)]
                for k in range(PRO * PTB):
                    st = nc.vector.bn_stats(stats[:, k // PTB, k % PTB, :], x_pass[k])
                st.then_inc(s_bn, 1)
                dve.wait_ge(s_bn, i + 1)
                dve.sem_inc(s_seen, 1)
                for k in range(PRO * PTB):
                    ag = nc.vector.bn_aggr(meanvar[:, k // PTB, k % PTB, :], stats[:, k // PTB, k % PTB, :])
                ag.then_inc(s_var, 1)
                dve.wait_ge(s_std, i + 1)
                nc.vector.reciprocal(rstd[:], std[:]).then_inc(s_rstd, 1)
                dve.wait_ge(s_rstd, i + 1)
                for s in range(PRO):
                    if later(i):
                        dve.wait_ge(s_xT, (i - 1) * PRO + s + 1)
                    for b in range(PTB):
                        norm = nc.vector.tensor_scalar(xn[:, s, b * P:(b + 1) * P], x_pass[s * PTB + b],
                                                       meanvar[:, s, b, 0:1], rstd[:, s, b:b + 1],
                                                       ALU.subtract, ALU.mult)
                    norm.then_inc(s_xn, 1)

            over_passes(dve, one_pass)

            dve.wait_ge(s_dstl, 16)
            nc.vector.tensor_copy(edge_rel[:], dst_i[:]).then_inc(s_dst, 1)
            dve.wait_ge(s_dst, 1)
            nc.vector.scalar_tensor_tensor(real_dst, edge_rel[:], float(FAR), edge_rel[:], ALU.is_lt, ALU.mult
                                           ).then_inc(s_dst, 1)
            nc.vector.tensor_reduce(lowest[:], edge_rel[:].rearrange("p (g c) -> p g c", c=GC), AX_X, ALU.min
                                    ).then_inc(s_dst, 1)
            dve.wait_ge(s_dst, 3)
            nc.vector.tensor_reduce(extremes[:, 0, :], real_dst.rearrange("p (g c) -> p g c", c=GC), AX_X, ALU.max
                                    ).then_inc(s_ext, 1)
            nc.vector.tensor_scalar(extremes[:, 1, :], lowest[:], -1.0, None, ALU.mult).then_inc(s_ext, 1)
            dve.wait_ge(s_w, 16 * (6 + LAYERS))
            nc.vector.tensor_tensor(bias_rz[:], bias[:, 0:2], bias[:, 3:5], ALU.add).then_inc(s_brz, 1)
            dve.wait_ge(s_const, 7)
            nc.vector.tensor_copy(node_iota[:], iota_i[:])
            nc.vector.tensor_copy(group_f[:], group_i[:])
            nc.vector.tensor_copy(tile_end[:], tile_end_i[:]).then_inc(s_dst, 1)

            dve.wait_ge(s_allext, 1)
            dve.wait_ge(s_dst, 4)
            nc.vector.tensor_scalar(lowest[:], allext[:, 1, :], -1.0, None, ALU.mult).then_inc(s_plan, 1)
            nc.vector.tensor_tensor(span[:], allext[0:1, 0, :], allext[0:1, 1, :], ALU.add).then_inc(s_plan, 1)
            dve.wait_ge(s_plan, 2)
            nc.vector.tensor_copy(plan[:, 0, :], lowest[0:1, :])
            nc.vector.tensor_copy(span_i[:], span[:]).then_inc(s_plan, 1)
            rel = edge_rel[:].rearrange("p (g c) -> p g c", c=GC)
            nc.vector.tensor_tensor(rel, rel, lowest[:].unsqueeze(2).to_broadcast([P, NG, GC]), ALU.subtract)
            nc.vector.scalar_tensor_tensor(needs[:], lowest[0:NT, :], tile_end[0:NT, 0:1], group_f[0:NT, :],
                                           ALU.is_lt, ALU.mult).then_inc(s_plan, 1)
            dve.wait_ge(s_plan, 4)
            nc.vector.tensor_scalar(windows_i[:], span_i[:], W.bit_length() - 1, None, ALU.logical_shift_right)
            nc.vector.tensor_reduce(needed[:], needs[:], AX_X, ALU.max).then_inc(s_plan, 1)
            dve.wait_ge(s_plan, 5)
            nc.vector.tensor_scalar(plan[:, 1, :], windows_i[:], 1, None, ALU.add).then_inc(s_plan, 1)
            nc.vector.tensor_copy(needed_i[:], needed[:]).then_inc(s_ready, 1)
            dve.wait_ge(s_plan, PLAN_STEPS)
            dve.wait_ge(s_readyrow, 16)
            dve.wait_ge(s_agg0, 1)
            prologue_scratch_free(dve)

            extra = dve.alloc_register("extra_windows")
            shifts = dve.alloc_register("extra_shifts")
            dve.reg_mov(extra, 0)
            dve.reg_mov(shifts, 0)
            next_tile = dve.alloc_register("next_tile")
            extra_low = dve.alloc_register("extra_window_low")
            columns = node_iota[:].unsqueeze(1).to_broadcast([P, GC, W])

            def window_onehot(out_, rel_):
                return nc.vector.tensor_tensor(out_, rel_.unsqueeze(2).to_broadcast([P, GC, W]), columns,
                                               ALU.is_equal)

            def make_onehot(layer, j, r):
                g = j * RING + r
                rel_g = edge_rel[:, bass.ds(g * GC, GC)]
                windows = dve.value_load(plan[0:1, 1, bass.ds(g, 1)], min_val=1, max_val=NPAD // W)
                with dve.If(windows > 1):
                    low = dve.value_load(plan[0:1, 0, bass.ds(g, 1)], min_val=0, max_val=NPAD - 1)
                    dve.reg_mov(extra_low, low)
                    dve.wait_ge(s_add, layer * NG + (j * RING + r - r % 2) + 1)
                    dve.reg_add(shifts, shifts, 1)
                    nc.vector.tensor_copy(xrel[:], rel_g).then_inc(s_xrel, 1)
                    with dve.Fori(1, windows):
                        dve.wait_ge(s_xrel, dve.snap(shifts))
                        dve.reg_add(shifts, shifts, 1)
                        nc.vector.tensor_scalar(xrel[:], xrel[:], -float(W), None, ALU.add).then_inc(s_xrel, 1)
                        dve.wait_ge(s_xrel, dve.snap(shifts))
                        window_onehot(xonehot[:], xrel[:]).then_inc(s_xoh, 1)
                        dve.reg_add(extra, extra, 1)
                        dve.wait_ge(s_xsum, dve.snap(extra))
                        dve.reg_add(extra_low, extra_low, W)
                        cols = aggT[:, bass.ds(dve.snap(extra_low, min_val=W, max_val=NPAD), W)]
                        nc.vector.tensor_tensor(cols, cols, XWINDOW, ALU.add).then_inc(s_xadd, 1)
                        dve.wait_ge(s_xadd, dve.snap(extra))
                dve.end_ifs()
                window_onehot(onehot[:, r % 2], rel_g).then_inc(s_oh, 1)

            def add_group(layer, j, r):
                g = j * RING + r
                low = dve.value_load(plan[0:1, 0, bass.ds(g, 1)], min_val=0, max_val=NPAD - 1)
                cols = aggT[:, bass.ds(low, W)]
                dve.wait_ge(s_sum, layer * NG + g + 1 + SUM_CREDIT)
                dve.wait_ge(s_add, layer * NG + g + 1)
                nc.vector.tensor_tensor(cols, cols, WINDOW[r % 2], ALU.add).then_inc(s_add, 1)

            def update_tile(layer, last, tile):
                t = layer * NT + tile
                nodes = bass.ds(tile * TN, TN)
                dve.wait_ge(s_hn, layer * (NT + 1) + tile + 1)
                dve.wait_ge(s_r, t + 1)
                nc.vector.scalar_tensor_tensor(blend[:], GATE_HN, bias[:, 5:6], gr[:], ALU.add, ALU.mult
                                               ).then_inc(s_rh, 1)
                dve.wait_ge(s_rh, t + 1)
                dve.wait_ge(s_gate, 3 * t + 2)
                nc.vector.tensor_tensor(npre[:], blend[:], GATE_IN, ALU.add).then_inc(s_npre, 1)
                dve.wait_ge(s_n, t + 1)
                nc.vector.tensor_tensor(blend[:], hT[:, nodes], gn[:], ALU.subtract).then_inc(s_blend, 1)
                dve.wait_ge(s_blend, 2 * t + 1)
                dve.wait_ge(s_z, t + 1)
                nc.vector.tensor_tensor(blend[:], blend[:], gz[:], ALU.mult).then_inc(s_blend, 1)
                dve.wait_ge(s_blend, 2 * t + 2)
                dve.wait_ge(s_mc, t + 1)
                nc.vector.tensor_tensor(hnew[:], blend[:], gn[:], ALU.add).then_inc(s_h, 1)
                dve.wait_ge(s_zero, t + 1)
                if last:
                    dve.wait_ge(s_m, t + 1)
                    dve.wait_ge(s_xres, 16 * (tile + 1))
                    nc.vector.tensor_tensor(mst[:], MSG, xres[:], ALU.add).then_inc(s_mc, 1)

            def layer_groups(layer, last):
                dve.reg_mov(next_tile, 0)
                with dve.Fori(0, NG // RING) as j:
                    for r in range(0, RING, 2):
                        make_onehot(layer, j, r)
                        make_onehot(layer, j, r + 1)
                        add_group(layer, j, r)
                        add_group(layer, j, r + 1)
                        done = j * RING + r + 2
                        with dve.While(lambda: dve.value_load(
                                tile_ready[0:1, bass.ds(dve.snap(next_tile, min_val=0, max_val=NT), 1)]) <= done):
                            update_tile(layer, last, dve.snap(next_tile, min_val=0, max_val=NT - 1))
                            dve.reg_add(next_tile, next_tile, 1)

            over_layers(dve, layer_groups)


def kernel(x, src, dst, L0_gnn_lin_w, L0_gnn_lin_b, L0_gnn_weight, L0_gnn_w_ih, L0_gnn_w_hh, L0_gnn_b_ih,
           L0_gnn_b_hh):
    import numpy as np
    import concourse.bacc as bacc
    from concourse.bass_utils import run_bass_kernel_spmd

    x = np.asarray(x)
    N, D = x.shape
    E = src.shape[0]
    whole = -(-N // (PTN * PRO)) * PTN * PRO
    tiles = -(-N // TN) * TN
    x_rows = np.zeros((whole, D), x.dtype)
    x_rows[:N] = x
    unit = GE * RING * IDX_HALVES
    edges = -(-E // unit) * unit

    def by_group(a, pad):
        whole = np.full(edges, pad, np.int32)
        whole[:E] = np.asarray(a)
        return np.ascontiguousarray(whole.reshape(edges // GE, P, GC).transpose(1, 0, 2).reshape(P, -1))

    def columns(b):
        return np.ascontiguousarray(np.asarray(b).reshape(-1, P).T)

    arrays = {
        "x": x_rows,
        "src": by_group(src, 0),
        "dst": by_group(dst, FAR),
        "lin_wT": np.ascontiguousarray(np.asarray(L0_gnn_lin_w).T),
        "lin_b": columns(L0_gnn_lin_b),
        "weight": np.ascontiguousarray(L0_gnn_weight),
        "w_ihT": np.ascontiguousarray(np.asarray(L0_gnn_w_ih).T),
        "w_hhT": np.ascontiguousarray(np.asarray(L0_gnn_w_hh).T),
        "b_ih": columns(L0_gnn_b_ih),
        "b_hh": columns(L0_gnn_b_hh),
    }
    nc = bacc.Bacc("TRN2", target_bir_lowering=False, num_devices=1)
    args = {n: nc.dram_tensor(f"in_{n}", a.shape, mybir.dt.from_np(a.dtype), kind="ExternalInput").ap()
            for n, a in arrays.items()}
    layers = arrays["weight"].shape[0]
    args["messages"] = [nc.dram_tensor(f"messages_{i}", (tiles if i else whole, D), F32, kind="Internal").ap() for i in range(layers)]
    args["out"] = nc.dram_tensor("out_rows", (tiles, D), F32, kind="ExternalOutput").ap()
    gated_graph_layers(nc, **args)
    r = run_bass_kernel_spmd(nc, [{f"in_{n}": a for n, a in arrays.items()}], core_ids=[0])
    return r.results[0]["out_rows"][:N]
```
